# Optimizing a Trainium2 kernel written in Bass

```python
import numpy as np
import jax
import jax.numpy as jnp

def _softmax(x, axis=-1):
    return jax.nn.softmax(x, axis=axis)

def _gelu(x):
    return jax.nn.gelu(x, approximate=True)

def _silu(x):
    return jax.nn.silu(x)

def _sigmoid(x):
    return jax.nn.sigmoid(x)

def _layernorm(x, axis=-1, eps=1e-05):
    m = jnp.mean(x, axis=axis, keepdims=True)
    v = jnp.var(x, axis=axis, keepdims=True)
    return (x - m) / jnp.sqrt(v + eps)

def _scatter_add(tgt, idx, src, axis=0):
    return tgt.at[idx].add(src)

def _segment_sum(src, seg, n):
    return jax.ops.segment_sum(src, seg, n)
kernel_name = 'mk_gnn_resnorm_d2_gnn_r8_fd6dff'

def setup_inputs(seed: int=0):
    np.random.seed(seed)
    _w = jnp.asarray

    def _rec_inputs():
        import jax
        import jax.numpy as jnp
        _gk = jax.random.key(seed)
        x = -0.0009044 + 1 * jax.random.normal(jax.random.fold_in(_gk, 1), (12500, 16), jnp.float32)
        src = jax.random.randint(jax.random.fold_in(_gk, 2), (400000,), 0, 12500, jnp.int32)
        dst = jax.random.randint(jax.random.fold_in(_gk, 3), (400000,), 0, 12500, jnp.int32)
        _o = jnp.argsort(dst, stable=True)
        src = src[_o]
        dst = dst[_o]
        edge_attr_16 = 0.000189758 + 1.00013 * jax.random.normal(jax.random.fold_in(_gk, 11), (400000, 16), jnp.float32)
        edge_attr_2 = jax.random.uniform(jax.random.fold_in(_gk, 12), (400000, 2), jnp.float32, 0.0, 1)
        return (x, src, dst, edge_attr_16, edge_attr_2)
    x, src, dst, edge_attr_16, edge_attr_2 = _rec_inputs()

    def _L0_gnn_setup():
        import jax, jax.numpy as jnp
        import numpy as np
        N_NODES = 12500
        N_EDGES = 400000
        N_CH = 16
        DT_MIN, DT_MAX = (0.01, 2.0)
        EPS = 1e-06
        key = jax.random.key(seed)
        k1, k2, k3 = jax.random.split(key, 3)
        u = jax.random.normal(k1, (N_NODES, N_CH), dtype=jnp.float32)
        edge_index = jax.random.randint(k2, (2, N_EDGES), 0, N_NODES, dtype=jnp.int64)
        edge_attr = jax.random.uniform(k3, (N_EDGES, 2), dtype=jnp.float32)
        dt = jnp.full((1,), 0.2, dtype=jnp.float32)
        g = jnp.full((1,), 9.81, dtype=jnp.float32)
        return {'u': u, 'edge_index': edge_index, 'edge_attr': edge_attr, 'dt': dt, 'g': g}
    _L0_gnn_all = _L0_gnn_setup()
    _L0_gnn_in = {k: v for k, v in _L0_gnn_all.items() if k in ('dt', 'g')}
    del _L0_gnn_all

    def _L1_gnn_setup():
        import jax, jax.numpy as jnp
        import numpy as np
        N_NODES = 12500
        N_EDGES = 400000
        D_FEAT = 16
        key = jax.random.key(seed)
        k1, k2, k3 = jax.random.split(key, 3)
        x = jax.random.normal(k1, (N_NODES, D_FEAT), dtype=jnp.float32)
        edge_index = jax.random.randint(k2, (2, N_EDGES), 0, N_NODES, dtype=jnp.int64)
        edge_attr = jax.random.normal(k3, (N_EDGES, D_FEAT), dtype=jnp.float32)
        return {'x': x, 'edge_index': edge_index, 'edge_attr': edge_attr}
    _L1_gnn_all = _L1_gnn_setup()
    _L1_gnn_in = {k: v for k, v in _L1_gnn_all.items() if k in ()}
    del _L1_gnn_all
    return {'x': x, 'src': src, 'dst': dst, 'edge_attr_16': edge_attr_16, 'edge_attr_2': edge_attr_2, 'L0_gnn_dt': _L0_gnn_in['dt'], 'L0_gnn_g': _L0_gnn_in['g']}

def reference(x, src, dst, edge_attr_16, edge_attr_2, L0_gnn_dt, L0_gnn_g):
    import jax
    import jax.numpy as jnp

    def _L0_gnn_ref(u, edge_index, edge_attr, dt, g):
        import jax, jax.numpy as jnp
        import numpy as np
        N_NODES = 12500
        N_EDGES = 400000
        N_CH = 16
        DT_MIN, DT_MAX = (0.01, 2.0)
        EPS = 1e-06
        src, dst = (edge_index[0], edge_index[1])
        N = u.shape[0]
        dx = jnp.maximum(edge_attr[:, 0], EPS)
        inv_dx = 1.0 / dx
        slope_e = edge_attr[:, 1] * inv_dx
        diff = (u[dst] - u[src]) * inv_dx[:, None]
        d1 = jax.ops.segment_sum(diff, dst, num_segments=N) - jax.ops.segment_sum(diff, src, num_segments=N)
        slope_edge = jnp.broadcast_to(slope_e[:, None], (slope_e.shape[0], u.shape[1]))
        S = jax.ops.segment_sum(slope_edge, dst, num_segments=N)
        dt_c = jnp.clip(dt, DT_MIN, DT_MAX)
        u_next = u - dt_c * (u * d1 + g * S)
        return u_next

    def _L1_gnn_ref(x, edge_index, edge_attr):
        import jax, jax.numpy as jnp
        import numpy as np
        N_NODES = 12500
        N_EDGES = 400000
        D_FEAT = 16
        nb_node = x.shape[0]
        dst = edge_index[1]
        sums = jax.ops.segment_sum(edge_attr, dst, num_segments=nb_node)
        counts = jax.ops.segment_sum(jnp.ones((edge_attr.shape[0],), dtype=edge_attr.dtype), dst, num_segments=nb_node)
        denom = jnp.where(counts > 0, counts, jnp.ones_like(counts))
        return sums / denom[:, None]
    edge_index = jnp.stack([src, dst])
    x = _layernorm(x + _L0_gnn_ref(x, edge_index, edge_attr_2, L0_gnn_dt, L0_gnn_g), axis=-1)
    x = _layernorm(x + _L1_gnn_ref(x, edge_index, edge_attr_16), axis=-1)
    return x

_drawn_inputs = setup_inputs


def setup_inputs(seed=0):
    import zlib

    import numpy as np

    out = dict(_drawn_inputs(seed))
    spreads = {}
    factors = {}
    for name, (base, spread) in spreads.items():
        noise = np.random.default_rng([zlib.crc32(name.encode()), seed]).standard_normal(out[name].shape)
        drawn = base * np.exp(spread * noise) if base else spread * noise
        out[name] = jnp.asarray(drawn.astype(out[name].dtype))
    for name, factor in factors.items():
        out[name] = (out[name] * factor).astype(out[name].dtype)
    return out
```

```python
import concourse.bass as bass
from concourse import mybir
from contextlib import ExitStack


def gnn_kernel(nc, x, src, dst, edge_attr_16, edge_attr_2, dt_in, g_in, out):
    f32, bf16, f16, i32 = mybir.dt.float32, mybir.dt.bfloat16, mybir.dt.float16, mybir.dt.int32
    ALU = mybir.AluOpType
    ACT = mybir.ActivationFunctionType
    AX = mybir.AxisListType.X
    ds = bass.ds

    P = 128
    NODES, F = x.shape
    EDGES = src.shape[0]
    J = 25
    CH = P * J
    C = EDGES // CH
    assert C * CH == EDGES and C % 2 == 1 and C <= P and C >= 3
    LO = P // F
    HI = -(-NODES // LO)
    HB = -(-HI // 4)
    HCOL = 4 * HB
    WIN = 128
    SPL = 3
    V = 2 * F + 2
    ONE = V - 1
    PADN = NODES + 140
    XR = 125
    XC = NODES // XR
    HT = -(-HI // P)
    FULLH = NODES // LO // P
    RING = 5
    EPS = 1e-5

    xparts_d = nc.dram_tensor("xparts_d", [PADN, SPL * F], bf16, kind="Internal").ap()

    src_v = src.rearrange("(c p j) -> c p j", p=P, j=J)
    dst_v = dst.rearrange("(c p j) -> c p j", p=P, j=J)
    dst_row = dst.rearrange("(c o e) -> c o e", o=1, e=CH)
    a2_v = edge_attr_2.rearrange("(c p j) t -> c p (j t)", p=P, j=J)
    a16_v = edge_attr_16.rearrange("(c p j) f -> c p (j f)", p=P, j=J)

    ctx = ExitStack()
    with ctx:
        def sb(name, shape, dt):
            return ctx.enter_context(nc.sbuf_tensor(name, shape, dt))

        def pb(name, shape, dt):
            return ctx.enter_context(nc.psum_tensor(name, shape, dt))

        def sem(name):
            return ctx.enter_context(nc.semaphore(name))

        src_i = sb("src_i", [P, 2, J], i32)
        dst_i = sb("dst_i", [P, 2, J], i32)
        dst_b = sb("dst_b", [P, 2, CH], i32)
        a2 = sb("a2", [P, 2, J * 2], f32)
        a16 = sb("a16", [P, 2, J * F], f32)
        x_src = sb("x_src", [P, 2, J * F], f32)
        xwin = sb("xwin", [P, 2, SPL * F], bf16)
        xwin_more = sb("xwin_more", [P, SPL * F], bf16)
        node_of_dst = sb("node_of_dst", [P, CH], bf16)
        dst_of_node = sb("dst_of_node", [P, J, WIN], bf16)
        dst_rel = sb("dst_rel", [P, J], f32)
        lo_i = sb("lo_i", [P, J], i32)
        hi_i = sb("hi_i", [P, J], i32)
        hi_f = sb("hi_f", [P, 2, J], f32)
        lo_hot = sb("lo_hot", [P, J, LO], bf16)
        dx = sb("dx", [P, J], f32)
        w = sb("w", [P, J], f32)
        x_dst = sb("x_dst", [P, J, F], f32)
        x_dst_more = sb("x_dst_more", [P, J, F], f32)
        pay = sb("pay", [P, J, V], f32)
        parts = sb("parts", [P, J, SPL, V], bf16)
        spread = sb("spread", [P, 2, J, SPL, LO, F], bf16)
        hi_hot = sb("hi_hot", [P, RING, HCOL], bf16)
        win_node = sb("win_node", [P, 1], f32)
        dst_sum = sb("dst_sum", [P, PADN], f32)
        col_h = sb("col_h", [P, HCOL], f16)
        col_i = sb("col_i", [P, P], i32)
        col_f = sb("col_f", [P, P], f32)
        row_i = sb("row_i", [P, 1], i32)
        row_f = sb("row_f", [P, 1], f32)
        ident = sb("ident", [P, P], f32)
        before = sb("before", [P, P], f32)
        join = sb("join", [P, SPL, V], f32)
        ones = sb("ones", [P, P], f32)
        zeros = sb("zeros", [P, P], bf16)
        lim = sb("lim", [P, 4], f32)
        more_i = sb("more_i", [P, 2], i32)
        more_f = sb("more_f", [P, 1], f32)
        base_diag = sb("base_diag", [P, P], f32)
        base_all = sb("base_all", [P, P], f32)
        node_all = sb("node_all", [P, P], f32)
        base_tab = sb("base_tab", [1, P], i32)
        more_tab = sb("more_tab", [1, P], i32)
        gdt = sb("gdt", [P, 4], f32)

        ps_src = pb("ps_src", [P, 4, 512], f32)
        ps_x = pb("ps_x", [P, 3, 512], f32)
        ps_w = pb("ps_w", [P, 512], f32)
        PER = 10

        x_rows = dst_sum[0:XR, 0:XC * F]
        x_rest = dst_sum[0:XR, XC * F:2 * XC * F].rearrange("p (n f) -> p n f", f=F)
        dst_all = dst_sum[0:C, 2 * XC * F:2 * XC * F + CH].bitcast(i32)
        x_split = spread[:, :, :, :, :, :].rearrange("p b j k l f -> p (b j k l f)")[0:XR, 0:XC * SPL * F] \
            .rearrange("p (n k f) -> p n k f", k=SPL, f=F)

        const_loaded = sem("const_loaded")
        gi_done = sem("gi_done")
        dve_step = sem("dve_step")
        tab_sum = sem("tab_sum")
        xparts_ready = sem("xparts_ready")
        xparts_stored = sem("xparts_stored")
        tables_ready = sem("tables_ready")
        src_loaded = [sem("src_loaded0"), sem("src_loaded1")]
        edges_loaded = [sem("edges_loaded0"), sem("edges_loaded1")]
        gather_begun = sem("gather_begun")
        gathered = [sem("gathered0"), sem("gathered1")]
        win_loaded = [sem("win_loaded0"), sem("win_loaded1")]
        more_loaded = sem("more_loaded")
        a16_copied = sem("a16_copied")
        node_hot_ready = sem("node_hot_ready")
        x_dst_ready = sem("x_dst_ready")
        parts_ready = sem("parts_ready")
        win_sum_ready = sem("win_sum_ready")
        chunk_ready = sem("chunk_ready")
        hi_hot_ready = sem("hi_hot_ready")
        hi_hot_free = sem("hi_hot_free")
        more_a = sem("more_a")
        more_hot = sem("more_hot")
        more_x = sem("more_x")
        more_b = sem("more_b")
        more_dhot = sem("more_dhot")
        more_sum = sem("more_sum")
        src_done = sem("src_done")
        fin_in = sem("fin_in")
        fin_ps = sem("fin_ps")
        fin_free = sem("fin_free")
        var_ready = sem("var_ready")
        std_ready = sem("std_ready")
        out_ready = sem("out_ready")
        out_done = sem("out_done")

        block = ctx.enter_context(nc.Block())

        PAIRS = (C - 1) // 2

        def bc(ap, axis, n):
            u = ap.unsqueeze(axis)
            shape = list(u.shape)
            shape[axis] = n
            return u.to_broadcast(shape)

        def later(base, g, first):
            return nc.s_assert_within(base + (g - first + 1) * WIN, 0, NODES - 1,
                                      skip_runtime_bounds_check_because="windows are counted up to the one that holds the greatest dst")

        def further_span(eng, c):
            return [eng.value_load(more_tab[0:1, ds(c + e, 1)], min_val=0, max_val=C * (NODES // WIN)) for e in range(2)]

        def further_in(eng, span, body):
            first, last = span
            with eng.If(last > first):
                with eng.Fori(first, last) as g:
                    body(g, first)

        def further(eng, c, body):
            further_in(eng, further_span(eng, c), body)

        big = spread[:, :, :, :, :, :].rearrange("p b j k l f -> p (b j k l f)").bitcast(f32)
        NF = HT * P
        sum_f = big[:, 0:HT * LO * V].rearrange("p (h l v) -> p h l v", h=HT, l=LO)
        o1 = HT * LO * V
        s_src = big[:, o1:o1 + NF].rearrange("p (h m) -> p h m", h=HT)
        u_all = big[:, o1 + NF:o1 + 2 * NF].rearrange("p (h m) -> p h m", h=HT)
        tmp_all = big[:, o1 + 2 * NF:o1 + 3 * NF].rearrange("p (h m) -> p h m", h=HT)
        src_t = hi_hot[:, :, :].rearrange("p r c -> p (r c)").bitcast(f32)[:, 0:HCOL]
        x_fin = hi_hot[:, :, :].rearrange("p r c -> p (r c)").bitcast(f32)[:, HCOL:HCOL + NF].rearrange("p (h m) -> p h m", h=HT)
        stat = dst_b[:, :, :].rearrange("p b e -> p (b e)").bitcast(f32)
        TAIL = NODES * F - FULLH * P * P
        TROW, TCOL = TAIL // P, TAIL % P

        A_AT, B_AT = 7, 22
        PIECE = {5: 0, 12: 1, 15: 2, 17: 3, 19: 4, 24: 5}
        NSTEP = 22

        def slot(j):
            return j % RING

        @block.sync
        def _(sp):
            sp.dma_start(x_rows, x.rearrange("(p n) f -> p (n f)", p=XR)).then_inc(const_loaded, 16)
            sp.dma_start(dst_all, dst.rearrange("(c e) -> c e", e=CH)).then_inc(const_loaded, 16)
            sp.dma_start(gdt[:, 0:1], dt_in.rearrange("(o t) -> o t", o=1).to_broadcast([P, 1])).then_inc(const_loaded, 16)
            sp.dma_start(gdt[:, 1:2], g_in.rearrange("(o t) -> o t", o=1).to_broadcast([P, 1])).then_inc(const_loaded, 16)

            def load(c, b):
                sp.dma_start(src_i[:, b, :], src_v[ds(c, 1), :, :].rearrange("o p j -> (o p) j")).then_inc(src_loaded[b], 16)
                sp.dma_start(dst_b[:, b, :], dst_row[ds(c, 1), :, :].rearrange("a o e -> (a o) e").to_broadcast([P, CH])).then_inc(edges_loaded[b], 16)
                sp.dma_start(dst_i[:, b, :], dst_v[ds(c, 1), :, :].rearrange("o p j -> (o p) j")).then_inc(edges_loaded[b], 16)
                sp.dma_start(a2[:, b, :], a2_v[ds(c, 1), :, :].rearrange("o p j -> (o p) j")).then_inc(edges_loaded[b], 16)
                sp.dma_start(a16[:, b, :], a16_v[ds(c, 1), :, :].rearrange("o p j -> (o p) j")).then_inc(edges_loaded[b], 16)

            load(0, 0)
            load(1, 1)
            with sp.Fori(0, PAIRS - 1) as i:
                for b in range(2):
                    sp.wait_ge(chunk_ready, i * 2 + b + 1)
                    load(i * 2 + (2 + b), b)
            sp.wait_ge(chunk_ready, C - 2)
            load(C - 1, 0)

            sp.wait_ge(fin_in, 1)
            sp.dma_start(x_fin[:, 0:FULLH, :], x.rearrange("n f -> (n f)")[0:FULLH * P * P].rearrange("(h p m) -> p h m", p=P, m=P)).then_inc(const_loaded, 16)
            xt = x.rearrange("n f -> (n f)")[FULLH * P * P:]
            sp.dma_start(x_fin[0:TROW, FULLH, :], xt[0:TROW * P].rearrange("(p m) -> p m", m=P)).then_inc(const_loaded, 16)
            if TCOL:
                sp.dma_start(x_fin[TROW:TROW + 1, FULLH, 0:TCOL], xt[TROW * P:].rearrange("(p m) -> p m", p=1)).then_inc(const_loaded, 16)
            sp.wait_ge(out_ready, 1)
            sp.dma_start(out.rearrange("n f -> (n f)")[0:FULLH * P * P].rearrange("(h p m) -> p h m", p=P, m=P), u_all[:, 0:FULLH, :]).then_inc(out_done, 16)
            ot = out.rearrange("n f -> (n f)")[FULLH * P * P:]
            sp.dma_start(ot[0:TROW * P].rearrange("(p m) -> p m", m=P), u_all[0:TROW, FULLH, :]).then_inc(out_done, 16)
            if TCOL:
                sp.dma_start(ot[TROW * P:].rearrange("(p m) -> p m", p=1), u_all[TROW:TROW + 1, FULLH, 0:TCOL]).then_inc(out_done, 16)
            sp.wait_ge(out_done, 16 * (2 + (TCOL > 0)))

        @block.gpsimd
        def _(pool):
            nc.gpsimd.iota(col_i[:, :], pattern=[[1, P]], base=0, channel_multiplier=0).then_inc(gi_done, 1)
            nc.gpsimd.iota(row_i[:, :], pattern=[[0, 1]], base=0, channel_multiplier=1).then_inc(gi_done, 1)
            nc.gpsimd.iota(col_h[:, :], pattern=[[1, HCOL]], base=0, channel_multiplier=0,
                           allow_small_or_imprecise_dtypes=True).then_inc(gi_done, 1)

            def gather(k, b):
                pool.wait_ge(src_loaded[b], k * 16 + 16)
                pool.sem_inc(gather_begun, 1)
                for j in range(J):
                    nc.gpsimd.indirect_dma_start(
                        x_src[:, b, j * F:(j + 1) * F], None, x[:, :],
                        bass.IndirectOffsetOnAxis(ap=src_i[:, b, j:j + 1], axis=0)).then_inc(gathered[b], 16)

            with pool.Fori(0, PAIRS) as i:
                for b in range(2):
                    gather(i, b)
            gather(PAIRS, 0)

        @block.scalar
        def _(act):
            act.wait_ge(xparts_ready, 1)
            act.dma_start(xparts_d[0:NODES, :].rearrange("(p n) q -> p (n q)", p=XR),
                          x_split.rearrange("p n k f -> p (n k f)")).then_inc(xparts_stored, 16)
            act.dma_start(xparts_d[NODES:NODES + P, :], zeros[:, 0:SPL * F]).then_inc(xparts_stored, 16)
            act.dma_start(xparts_d[NODES + P:PADN, :], zeros[0:PADN - NODES - P, 0:SPL * F]).then_inc(xparts_stored, 16)
            act.wait_ge(xparts_stored, 48)
            act.wait_ge(tables_ready, 1)

            def windows(c, k, b):
                base = act.value_load(base_tab[0:1, ds(c, 1)], min_val=0, max_val=NODES - 1)
                act.dma_start(xwin[:, b, :], xparts_d[ds(base, WIN), :]).then_inc(win_loaded[b], 16)

                def more(g, first):
                    act.wait_ge(more_x, g + 1)
                    act.dma_start(xwin_more[:, :], xparts_d[ds(later(base, g, first), WIN), :]).then_inc(more_loaded, 16)

                further(act, c, more)
                act.wait_ge(edges_loaded[b], k * 64 + 64)
                act.wait_ge(parts_ready, c)
                nc.scalar.copy(pay[:, :, F + 1:2 * F + 1], a16[:, b, :].rearrange("p (j f) -> p j f", f=F)).then_inc(a16_copied, 1)

            windows(0, 0, 0)
            windows(1, 0, 1)
            with act.Fori(0, PAIRS - 1) as i:
                for b in range(2):
                    act.wait_ge(x_dst_ready, i * 2 + b + 1)
                    windows(i * 2 + (2 + b), i + 1, b)
            act.wait_ge(x_dst_ready, C - 2)
            windows(C - 1, PAIRS, 0)

            for n in range(2):
                act.wait_ge(var_ready, n + 1)
                nc.scalar.activation(stat[:, NF // F:2 * NF // F], stat[:, 0:NF // F], ACT.Sqrt, bias=lim[:, 3:4]).then_inc(std_ready, 1)

        @block.tensor
        def _(pe):
            pe.wait_ge(tab_sum, 1)
            nc.tensor.matmul(ps_w[0:1, 0:C], lim[0:C, 0:1], ident[0:C, 0:C], start=True, stop=True)
            nc.tensor.matmul(ps_w[0:1, P:P + C + 1], more_f[0:C, :], before[0:C, 0:C + 1], start=True, stop=True)
            nc.tensor.matmul(ps_w[:, 2 * P:2 * P + C], ones[0:C, :], base_diag[0:C, 0:C], start=True, stop=True).then_inc(tab_sum, 1)
            pe.wait_ge(gi_done, 3)
            for q in range(4):
                nc.tensor.matmul(ps_src[:, q, 0:HB], zeros[:, :], col_h[:, q * HB:(q + 1) * HB], start=True, stop=False)

            def x_of_dst(c, k, b):
                pe.wait_ge(win_loaded[b], k * 16 + 16)
                pe.wait_ge(node_hot_ready, c + 1)
                for j in range(J):
                    last = nc.tensor.matmul(ps_x[:, j // PER, (j % PER) * SPL * F:(j % PER + 1) * SPL * F],
                                            node_of_dst[:, j * P:(j + 1) * P], xwin[:, b, :], start=True, stop=True)
                last.then_inc(x_dst_ready, 1)

                def more(g, first):
                    pe.wait_ge(more_loaded, g * 16 + 16)
                    pe.wait_ge(more_hot, g + 1)
                    for j in range(J):
                        last = nc.tensor.matmul(ps_x[:, j // PER, (j % PER) * SPL * F:(j % PER + 1) * SPL * F],
                                                node_of_dst[:, j * P:(j + 1) * P], xwin_more[:, :], start=True, stop=True)
                    last.then_inc(more_x, 1)

                further(pe, c, more)

            def window_sums(c):
                pe.wait_ge(parts_ready, c + 1)

                def sums():
                    for j in range(J):
                        last = nc.tensor.matmul(ps_w[0:SPL * V, 0:WIN], parts[:, j, :, :].rearrange("p k v -> p (k v)"),
                                                dst_of_node[:, j, :], start=(j == 0), stop=(j == J - 1))
                    return last

                sums().then_inc(win_sum_ready, 1)

                def more(g, first):
                    pe.wait_ge(more_dhot, g + 1)
                    sums().then_inc(more_sum, 1)

                further(pe, c, more)

            def tile(c, b, j, stop):
                pe.wait_ge(hi_hot_ready, c * J + j + 1)
                for q in range(4):
                    for k in range(SPL):
                        last = nc.tensor.matmul(ps_src[:, q, 0:HB], spread[:, b, j, k, :, :].rearrange("p l f -> p (l f)"),
                                                hi_hot[:, slot(j), q * HB:(q + 1) * HB], start=False, stop=stop and k == SPL - 1)
                last.then_inc(hi_hot_free, 1)

            def stage(c, k_next, b, last):
                pe.wait_ge(chunk_ready, c + 1)
                for j in range(J):
                    tile(c, b, j, last and j == J - 1)
                    if j == A_AT and not last:
                        x_of_dst(c + 1, k_next, 1 - b)
                    if j == B_AT and not last:
                        window_sums(c + 1)

            x_of_dst(0, 0, 0)
            window_sums(0)
            with pe.Fori(0, PAIRS) as i:
                stage(i * 2, i, 0, False)
                stage(i * 2 + 1, i + 1, 1, False)
            stage(C - 1, 0, 0, True)
            nc.tensor.matmul(ps_w[0:1, 0:1], ident[:, 0:1], ident[:, 0:1], start=True, stop=True).then_inc(src_done, 1)

            pe.wait_ge(fin_in, 1)
            for h in range(HT):
                n = min(P, HCOL - h * P)
                if h >= 1:
                    pe.wait_ge(fin_free, h)
                nc.tensor.transpose(ps_x[0:n, 0, 0:P], src_t[:, h * P:h * P + n], ident[:, :])
                for l in range(LO):
                    last = nc.tensor.matmul(ps_x[0:n, 1, l * V:(l + 1) * V],
                                            dst_sum[0:SPL * V, h * P * LO + l:h * P * LO + l + (n - 1) * LO + 1:LO],
                                            join[0:SPL * V, 0, :], start=True, stop=True)
                last.then_inc(fin_ps, 1)

        @block.vector
        def _(dve):
            v = nc.vector
            count = [0]

            def step(ins):
                count[0] += 1
                ins.then_inc(dve_step, 1)

            def settle(base=0):
                dve.wait_ge(dve_step, base + count[0])

            step(v.memset(zeros[:, :], 0.0))
            step(v.memset(ones[:, :], 1.0))
            v.memset(win_node[:, :], 0.0).then_inc(hi_hot_free, RING)
            step(v.memset(lim[:, :], 0.0))
            v.memset(dx[:, :], 0.0).then_inc(more_x, 1)
            v.memset(w[:, :], 0.0).then_inc(more_a, 1)
            v.memset(dst_rel[:, :], 0.0).then_inc(more_b, 1)
            dve.wait_ge(gi_done, 3)
            step(v.tensor_copy(col_f[:, :], col_i[:, :]))
            step(v.tensor_copy(row_f[:, :], row_i[:, :]))
            step(v.memset(parts[:, :, :, :], 0.0))
            settle()
            step(v.memset(lim[:, 3:4], EPS))
            step(v.memset(parts[:, :, 0, ONE:ONE + 1], 1.0))
            step(v.tensor_scalar(ident[:, :], col_f[:, :], row_f[:, 0:1], None, ALU.is_equal))
            step(v.tensor_scalar(before[:, :], col_f[:, :], row_f[:, 0:1], None, ALU.is_gt))
            for k in range(SPL):
                step(v.tensor_scalar(join[:, k, :], col_f[:, 0:V], float(k * V), row_f[:, 0:1], ALU.add, ALU.is_equal))
            settle()
            step(v.tensor_tensor(join[:, 0, :], join[:, 0, :], join[:, 1, :], ALU.add))
            settle()
            step(v.tensor_tensor(join[:, 0, :], join[:, 0, :], join[:, 2, :], ALU.add))

            dve.wait_ge(const_loaded, 64)
            xr = x_rows.rearrange("p (n f) -> p n f", f=F)
            step(v.tensor_copy(x_split[:, :, 0, :], xr))
            settle()
            step(v.tensor_tensor(x_rest, xr, x_split[:, :, 0, :], ALU.subtract))
            settle()
            step(v.tensor_copy(x_split[:, :, 1, :], x_rest))
            settle()
            v.tensor_tensor(x_split[:, :, 2, :], x_rest, x_split[:, :, 1, :], ALU.subtract).then_inc(xparts_ready, 1)

            step(v.tensor_reduce(lim[0:C, 0:1], dst_all, AX, ALU.min))
            step(v.tensor_reduce(lim[0:C, 1:2], dst_all, AX, ALU.max))
            settle()
            step(v.tensor_tensor(more_i[0:C, 0:1], lim[0:C, 1:2], lim[0:C, 0:1], ALU.subtract))
            step(v.tensor_scalar(base_diag[0:C, 0:C], ident[0:C, 0:C], lim[0:C, 0:1], None, ALU.mult))
            settle()
            step(v.tensor_single_scalar(more_i[0:C, 1:2], more_i[0:C, 0:1], 7, ALU.arith_shift_right))
            settle()
            v.tensor_copy(more_f[0:C, :], more_i[0:C, 1:2]).then_inc(tab_sum, 1)
            dve.wait_ge(xparts_ready, 1)
            step(v.memset(dst_sum[:, :], 0.0))
            dve.wait_ge(tab_sum, 2)
            step(v.tensor_copy(base_tab[0:1, 0:C], ps_w[0:1, 0:C]))
            step(v.tensor_copy(more_tab[0:1, 0:C + 1], ps_w[0:1, P:P + C + 1]))
            step(v.tensor_copy(base_all[:, 0:C], ps_w[:, 2 * P:2 * P + C]))
            settle()
            v.tensor_scalar(node_all[:, 0:C], base_all[:, 0:C], row_f[:, 0:1], None, ALU.add).then_inc(tables_ready, 1)
            dve.wait_ge(tables_ready, 1)
            dve.wait_ge(xparts_stored, 48)
            start = count[0]

            def x_dst_add(out_t):
                for q in range(3):
                    n = min(PER, J - q * PER)
                    yield v.tensor_reduce(out_t[:, q * PER:q * PER + n, :],
                                          ps_x[:, q, 0:n * SPL * F].rearrange("p (j k f) -> p j f k", k=SPL, f=F), AX, ALU.add)

            def prepare(n, k, b, piece):
                def settle_here():
                    dve.wait_ge(dve_step, start + n * NSTEP + count[0])

                s = dst_b[:, b, :].rearrange("p (e j) -> p j e", j=J)
                hot = node_of_dst[:, :].rearrange("p (j e) -> p j e", j=J)
                if piece == 0:
                    count[0] = 0
                    dve.wait_ge(src_loaded[b], k * 16 + 16)
                    dve.wait_ge(edges_loaded[b], k * 64 + 64)
                    v.tensor_scalar(hot, s, node_all[:, ds(n, 1)], None, ALU.is_equal).then_inc(node_hot_ready, 1)
                    step(v.tensor_scalar(dst_rel[:, :], dst_i[:, b, :], base_all[:, ds(n, 1)], None, ALU.subtract))
                    step(v.tensor_single_scalar(lo_i[:, :], src_i[:, b, :], LO - 1, ALU.bitwise_and))
                    step(v.tensor_single_scalar(hi_i[:, :], src_i[:, b, :], 3, ALU.logical_shift_right))
                    step(v.tensor_scalar(dx[:, :], a2[:, b, 0:2 * J:2], 1e-6, None, ALU.max))
                    settle_here()
                    step(v.tensor_copy(hi_f[:, b, :], hi_i[:, :]))
                    step(v.tensor_tensor(lo_hot[:, :, :], bc(lo_i[:, :], 2, LO), bc(col_i[:, 0:LO], 1, J), ALU.is_equal))
                    step(v.tensor_tensor(dst_of_node[:, :, :], bc(dst_rel[:, :], 2, WIN), bc(col_f[:, 0:WIN], 1, J), ALU.is_equal))
                    step(v.reciprocal(w[:, :], dx[:, :]))
                if piece == 1:
                    span = further_span(dve, n)
                    dve.wait_ge(x_dst_ready, n + 1)
                    for ins in x_dst_add(x_dst):
                        step(ins)
                    settle_here()

                    def more_(g, first):
                        settle_here()
                        dve.wait_ge(more_a, g * 5 + 1)
                        v.tensor_scalar(win_node[:, :], win_node[:, :], float(WIN), None, ALU.add).then_inc(more_a, 1)
                        dve.wait_ge(more_a, g * 5 + 2)
                        v.tensor_scalar(hot, s, win_node[:, :], None, ALU.is_equal).then_inc(more_hot, 1)
                        dve.wait_ge(more_x, g + 2)
                        for ins in x_dst_add(x_dst_more):
                            ins.then_inc(more_a, 1)
                        dve.wait_ge(more_a, g * 5 + 5)
                        v.tensor_tensor(x_dst[:, :, :], x_dst[:, :, :], x_dst_more[:, :, :], ALU.add).then_inc(more_a, 1)

                    step(v.tensor_scalar(win_node[:, :], node_all[:, ds(n, 1)], 0.0, None, ALU.add))
                    further_in(dve, span, more_)
                    dve.wait_ge(more_a, span[1] * 5 + 1)

                    dve.wait_ge(gathered[b], (k + 1) * 16 * J)
                    xs = x_src[:, b, :].rearrange("p (j f) -> p j f", f=F)
                    step(v.tensor_tensor(x_dst[:, :, :], x_dst[:, :, :], xs, ALU.subtract))
                    dve.wait_ge(a16_copied, n + 1)
                    step(v.tensor_tensor(pay[:, :, F], a2[:, b, 1:2 * J:2], w[:, :], ALU.mult))
                    settle_here()
                    step(v.tensor_tensor(pay[:, :, 0:F], x_dst[:, :, :], bc(w[:, :], 2, F), ALU.mult))
                    settle_here()
                    rest = pay[:, :, 0:ONE]
                    step(v.tensor_copy(parts[:, :, 0, 0:ONE], rest))
                    settle_here()
                    step(v.tensor_tensor(rest, rest, parts[:, :, 0, 0:ONE], ALU.subtract))
                    settle_here()
                    step(v.tensor_copy(parts[:, :, 1, 0:ONE], rest))
                    settle_here()
                    v.tensor_tensor(parts[:, :, 2, 0:ONE], rest, parts[:, :, 1, 0:ONE], ALU.subtract).then_inc(parts_ready, 1)
                if 2 <= piece <= 4:
                    q = piece - 2
                    if q == 0:
                        dve.wait_ge(hi_hot_free, (n - 1) * J + RING) if not (isinstance(n, int) and n == 0) else None
                        dve.wait_ge(parts_ready, n + 1)
                    if q == SPL - 1:
                        settle_here()
                    ins = v.tensor_tensor(spread[:, b, :, q, :, :], bc(lo_hot[:, :, :], 3, F), bc(parts[:, :, q, 0:F], 2, LO), ALU.mult)
                    if q == SPL - 1:
                        ins.then_inc(chunk_ready, 1)
                    else:
                        step(ins)
                if piece == 5:
                    span = further_span(dve, n)
                    base = dve.value_load(base_tab[0:1, ds(n, 1)], min_val=0, max_val=NODES - 1)
                    dve.wait_ge(win_sum_ready, n + 1)
                    win = dst_sum[0:SPL * V, ds(base, WIN)]
                    step(v.tensor_tensor(win, win, ps_w[0:SPL * V, 0:WIN], ALU.add))

                    def more(g, first):
                        settle_here()
                        dve.wait_ge(more_b, g * 2 + 1)
                        v.tensor_scalar(dst_rel[:, :], dst_rel[:, :], float(-WIN), None, ALU.add).then_inc(more_b, 1)
                        dve.wait_ge(more_b, g * 2 + 2)
                        v.tensor_tensor(dst_of_node[:, :, :], bc(dst_rel[:, :], 2, WIN), bc(col_f[:, 0:WIN], 1, J), ALU.is_equal).then_inc(more_dhot, 1)
                        dve.wait_ge(more_sum, g + 1)
                        wn = dst_sum[0:SPL * V, ds(later(base, g, first), WIN)]
                        v.tensor_tensor(wn, wn, ps_w[0:SPL * V, 0:WIN], ALU.add).then_inc(more_b, 1)

                    further_in(dve, span, more)
                    settle_here()
                    dve.wait_ge(more_b, span[1] * 2 + 1)
                    step(v.memset(win_node[:, :], 0.0))
                    assert count[0] == NSTEP, count[0]

            for piece in range(6):
                prepare(0, 0, 0, piece)

            def one_hot(c, b, j):
                dve.wait_ge(hi_hot_free, c * J + j + 1)
                v.tensor_scalar(hi_hot[:, slot(j), :], col_h[:, :], hi_f[:, b, j:j + 1], None, ALU.is_equal).then_inc(hi_hot_ready, 1)

            def stage(c, k_next, b, last):
                for j in range(J):
                    one_hot(c, b, j)
                    if j in PIECE and not last:
                        prepare(c + 1, k_next, 1 - b, PIECE[j])

            with dve.Fori(0, PAIRS) as i:
                stage(i * 2, i, 0, False)
                stage(i * 2 + 1, i + 1, 1, False)
            stage(C - 1, 0, 0, True)

            fin = [0]
            fin_base = start + C * NSTEP

            def fstep(ins):
                fin[0] += 1
                ins.then_inc(dve_step, 1)

            def fsettle():
                dve.wait_ge(dve_step, fin_base + fin[0])

            dve.wait_ge(src_done, 1)
            dve.wait_ge(hi_hot_free, C * J + RING)
            fstep(v.memset(x_fin[:, FULLH, :], 0.0))
            fstep(v.memset(big[:, :], 0.0))
            for q in range(3):
                fstep(v.tensor_copy(src_t[:, q * HB:(q + 1) * HB], ps_src[:, q, 0:HB]))
            fsettle()
            v.tensor_copy(src_t[:, 3 * HB:HCOL], ps_src[:, 3, 0:HB]).then_inc(fin_in, 1)
            for h in range(HT):
                n = min(P, HCOL - h * P)
                dve.wait_ge(fin_ps, h + 1)
                fstep(v.tensor_copy(s_src[0:n, h, :], ps_x[0:n, 0, 0:P]))
                fsettle()
                v.tensor_copy(sum_f[0:n, h, :, :], ps_x[0:n, 1, 0:LO * V].rearrange("p (l v) -> p l v", l=LO)).then_inc(fin_free, 1)
            dve.wait_ge(fin_free, HT)
            dve.wait_ge(const_loaded, 64 + 16 * (2 + (TCOL > 0)))

            G = HT * LO
            nodes = lambda t: t.rearrange("p h (l f) -> p (h l) f", f=F)
            sums = sum_f.rearrange("p h l v -> p (h l) v")
            u3, x3, t3, s3 = nodes(u_all), nodes(x_fin), nodes(tmp_all), nodes(s_src)
            var, std, cnt, mean, rstd = (stat[:, q * G:(q + 1) * G] for q in range(5))

            def op(ins):
                fstep(ins)
                fsettle()

            op(v.tensor_scalar(gdt[:, 2:3], gdt[:, 0:1], 0.01, 2.0, ALU.max, ALU.min))
            op(v.tensor_tensor(t3, sums[:, :, 0:F], s3, ALU.subtract))
            op(v.tensor_tensor(t3, t3, x3, ALU.mult))
            op(v.tensor_scalar(mean, sums[:, :, F], gdt[:, 1:2], None, ALU.mult))
            op(v.tensor_tensor(t3, t3, bc(mean, 2, F), ALU.add))
            op(v.tensor_scalar(t3, t3, gdt[:, 2:3], None, ALU.mult))
            op(v.tensor_tensor(t3, x3, t3, ALU.subtract))
            op(v.tensor_tensor(u3, x3, t3, ALU.add))

            def layer_norm():
                op(v.tensor_reduce(mean, u3, AX, ALU.add))
                op(v.tensor_scalar(mean, mean, 1.0 / F, None, ALU.mult))
                op(v.tensor_tensor(u3, u3, bc(mean, 2, F), ALU.subtract))
                op(v.tensor_tensor(t3, u3, u3, ALU.mult))
                op(v.tensor_reduce(var, t3, AX, ALU.add))
                v.tensor_scalar(var, var, 1.0 / F, None, ALU.mult).then_inc(var_ready, 1)

            layer_norm()
            dve.wait_ge(std_ready, 1)
            op(v.reciprocal(rstd, std))
            op(v.tensor_tensor(u3, u3, bc(rstd, 2, F), ALU.mult))
            op(v.tensor_scalar(cnt, sums[:, :, ONE], 1.0, None, ALU.max))
            op(v.reciprocal(cnt, cnt))
            op(v.tensor_tensor(t3, sums[:, :, F + 1:2 * F + 1], bc(cnt, 2, F), ALU.mult))
            op(v.tensor_tensor(u3, u3, t3, ALU.add))
            layer_norm()
            dve.wait_ge(std_ready, 2)
            op(v.reciprocal(rstd, std))
            v.tensor_tensor(u3, u3, bc(rstd, 2, F), ALU.mult).then_inc(out_ready, 1)


_INS = ['x', 'src', 'dst', 'edge_attr_16', 'edge_attr_2', 'L0_gnn_dt', 'L0_gnn_g']


def kernel(**inputs):
    import numpy as _np
    import concourse.bacc as _bacc
    from concourse import mybir as _mybir
    from concourse.bass_utils import run_bass_kernel_spmd as _run

    nc = _bacc.Bacc("TRN2", target_bir_lowering=False, num_devices=1)
    arrays, args = {}, []
    for name in _INS:
        a = _np.ascontiguousarray(inputs[name])
        arrays[f"in_{name}_dram"] = a
        args.append(nc.dram_tensor(f"in_{name}_dram", a.shape, _mybir.dt.from_np(a.dtype), kind="ExternalInput").ap())
    out = nc.dram_tensor("out_0_dram", inputs['x'].shape, _mybir.dt.float32, kind="ExternalOutput").ap()
    gnn_kernel(nc, *args, out)
    r = _run(nc, [arrays], core_ids=[0])
    return r.results[0]["out_0_dram"]
```

```python
import concourse.bass as bass
from concourse import mybir
from contextlib import ExitStack


def gnn_kernel(nc, x, src, dst, edge_attr_16, edge_attr_2, dt_in, g_in, out):
    f32, bf16, f16, i32 = mybir.dt.float32, mybir.dt.bfloat16, mybir.dt.float16, mybir.dt.int32
    ALU = mybir.AluOpType
    ACT = mybir.ActivationFunctionType
    AX = mybir.AxisListType.X
    ds = bass.ds

    P = 128
    NODES, F = x.shape
    EDGES = src.shape[0]
    J = 25
    CH = P * J
    C = EDGES // CH
    assert C * CH == EDGES and C % 2 == 1 and C <= P and C >= 7
    LO = P // F
    HI = -(-NODES // LO)
    HB = -(-HI // 4)
    HCOL = 4 * HB
    WIN = 128
    SPL = 3
    HLV = 2
    V = 2 * F + 2
    ONE = V - 1
    PADN = NODES + 140
    XR = 125
    XC = NODES // XR
    HT = -(-HI // P)
    FULLH = NODES // LO // P
    RING = 10
    S = 5
    JP = J - S
    assert NODES + P <= 1 << 14
    EPS = 1e-5

    xparts_d = nc.dram_tensor("xparts_d", [PADN, SPL * F], bf16, kind="Internal").ap()

    pool_sum_d = nc.dram_tensor("pool_sum_d", [NODES + P, F], f32, kind="Internal").ap()

    src_v = src.rearrange("(c p j) -> c p j", p=P, j=J)
    dst_v = dst.rearrange("(c p j) -> c p j", p=P, j=J)
    a2_v = edge_attr_2.rearrange("(c p j) t -> c p (j t)", p=P, j=J)
    a16_v = edge_attr_16.rearrange("(c p j) f -> c p (j f)", p=P, j=J)

    ctx = ExitStack()
    with ctx:
        def sb(name, shape, dt):
            return ctx.enter_context(nc.sbuf_tensor(name, shape, dt))

        def pb(name, shape, dt):
            return ctx.enter_context(nc.psum_tensor(name, shape, dt))

        def sem(name):
            return ctx.enter_context(nc.semaphore(name))

        src_i = sb("src_i", [P, 2, J], i32)
        dst_i = sb("dst_i", [P, 2, J], i32)
        a2 = sb("a2", [P, 2, J * 2], f32)
        a16 = sb("a16", [P, 2, J * F], f32)
        x_src = sb("x_src", [P, 2, J * F], f32)
        xwin = sb("xwin", [P, 2, SPL * F], bf16)
        xwin_more = sb("xwin_more", [P, SPL * F], bf16)
        node_of_dst = sb("node_of_dst", [P, J, P], bf16)
        more_node = sb("more_node", [P, J, WIN], bf16)
        more_rel = sb("more_rel", [P, J], f32)
        dst_of_node = sb("dst_of_node", [P, J, WIN], bf16)
        dst_rel = sb("dst_rel", [P, J], f32)
        lo_i = sb("lo_i", [P, J], i32)
        hi_i = sb("hi_i", [P, J], i32)
        hi_f = sb("hi_f", [P, 2, J], f32)
        lo_hot = sb("lo_hot", [P, JP, LO], f16)
        lo_rows = sb("lo_rows", [P, JP, LO, F], f16)
        dx = sb("dx", [P, J], f32)
        w = sb("w", [P, J], f32)
        x_dst = sb("x_dst", [P, J, F], f32)
        x_dst_more = sb("x_dst_more", [P, J, F], f32)
        left = sb("left", [P, J, ONE], f32)
        pay = sb("pay", [P, J, V], f32)
        parts = sb("parts", [P, J, SPL, V], bf16)
        halves = sb("halves", [P, JP, HLV, F], f16)
        spread = sb("spread", [P, 2, JP, HLV, LO, F], f16)
        top = sb("top", [P, JP], f32)
        scale = sb("scale", [P, 2, JP], f32)
        unscale = sb("unscale", [P, JP], f32)
        scaled = sb("scaled", [P, JP, F], f32)
        src_f = sb("src_f", [P, 2, S], f32)
        src_f16 = sb("src_f16", [P, S, 2], f16)
        same_src = sb("same_src", [P, S, P], bf16)
        weight_i = sb("weight_i", [P, 1], i32)
        weight = sb("weight", [P, 1], bf16)
        reach = sb("reach", [P, 1], f32)
        spare_row = sb("spare_row", [P, 1], f32)
        merged = sb("merged", [P, 2, S, F + 1], f32)
        is_later = sb("is_later", [P, S], f32)
        row_of = sb("row_of", [P, 2, S], i32)
        hi_hot = sb("hi_hot", [P, RING, HCOL], bf16)
        dst_sum = sb("dst_sum", [P, PADN], f32)
        col_h = sb("col_h", [P, HCOL], f16)
        col_i = sb("col_i", [P, P], i32)
        col_f = sb("col_f", [P, P], f32)
        row_i = sb("row_i", [P, 1], i32)
        row_f = sb("row_f", [P, 1], f32)
        ident = sb("ident", [P, P], f32)
        ident_b = sb("ident_b", [P, P], bf16)
        x_fin = sb("x_fin", [P, HT, P], f32)
        pool_sum = sb("pool_sum", [P, HT, P], f32)
        before = sb("before", [P, P], f32)
        ones = sb("ones", [P, P], f32)
        zeros = sb("zeros", [P, P], bf16)
        lim = sb("lim", [P, 4], f32)
        more_i = sb("more_i", [P, 2], i32)
        more_f = sb("more_f", [P, 1], f32)
        base_diag = sb("base_diag", [P, P], f32)
        base_all = sb("base_all", [P, P], f32)
        base_tab = sb("base_tab", [1, P], i32)
        more_tab = sb("more_tab", [1, P], i32)
        gdt = sb("gdt", [P, 4], f32)

        ps_src = pb("ps_src", [P, 4, 512], f32)
        ps_x = pb("ps_x", [P, 3, 512], f32)
        ps_w = pb("ps_w", [P, 512], f32)
        PER = 10
        TPB = 512 * 4 // (P * 2)
        turned = ps_x[:, :, :].rearrange("p q n -> p (q n)").bitcast(bf16).rearrange("p (j e) -> p j e", e=P)
        ps_rows = ps_x[:, 0:2, :].rearrange("p q n -> p (q n)")[:, 0:S * P]
        ps_merged = ps_x[:, 2, 0:S * (F + 1)].rearrange("p (s v) -> p s v", s=S)
        turned_last = ps_w[:, 0:P // 2].bitcast(bf16)

        x_rows = dst_sum[0:XR, 0:XC * F]
        x_rest = dst_sum[0:XR, XC * F:2 * XC * F].rearrange("p (n f) -> p n f", f=F)
        CLEAR = (2 * XC * F, 2 * XC * F + CH)
        dst_all = dst_sum[0:C, CLEAR[0]:CLEAR[1]].bitcast(i32)
        x_split = spread[:, :, :, :, :, :].rearrange("p b j k l f -> p (b j k l f)").bitcast(bf16)[0:XR, 0:XC * SPL * F] \
            .rearrange("p (n k f) -> p n k f", k=SPL, f=F)

        const_loaded = sem("const_loaded")
        gi_done = sem("gi_done")
        dve_step = sem("dve_step")
        tab_sum = sem("tab_sum")
        xparts_ready = sem("xparts_ready")
        xparts_stored = sem("xparts_stored")
        tables_ready = sem("tables_ready")
        src_loaded = [sem("src_loaded0"), sem("src_loaded1")]
        edges_loaded = [sem("edges_loaded0"), sem("edges_loaded1")]
        same_ready = sem("same_ready")
        rows_of_src = sem("rows_of_src")
        merge_done = sem("merge_done")
        merged_ready = sem("merged_ready")
        later_ready = sem("later_ready")
        row_ready = sem("row_ready")
        rows_taken = sem("rows_taken")
        scatter_begun = sem("scatter_begun")
        scatter_done = sem("scatter_done")
        sums_clear = sem("sums_clear")
        src_in = sem("src_in")
        fin_dst = sem("fin_dst")
        fin_count = sem("fin_count")
        attr_ready = sem("attr_ready")
        scatter_zero = sem("scatter_zero")
        scatter_clear = sem("scatter_clear")
        pool_sum_loaded = sem("pool_sum_loaded")
        weight_ready = sem("weight_ready")
        gather_begun = sem("gather_begun")
        gathered = [sem("gathered0"), sem("gathered1")]
        win_loaded = [sem("win_loaded0"), sem("win_loaded1")]
        more_loaded = sem("more_loaded")
        a16_copied = sem("a16_copied")
        node_hot_ready = sem("node_hot_ready")
        x_dst_ready = sem("x_dst_ready")
        parts_ready = sem("parts_ready")
        win_sum_ready = sem("win_sum_ready")
        chunk_ready = sem("chunk_ready")
        hi_hot_ready = sem("hi_hot_ready")
        hi_hot_free = sem("hi_hot_free")
        dst_hot_ready = sem("dst_hot_ready")
        hot_turned = sem("hot_turned")
        lo_ready = sem("lo_ready")
        lo_rows_ready = sem("lo_rows_ready")
        pay_ready = sem("pay_ready")
        part0_ready = sem("part0_ready")
        left_ready = sem("left_ready")
        part1_ready = sem("part1_ready")
        scaled_ready = sem("scaled_ready")
        half0_ready = sem("half0_ready")
        more_turned = sem("more_turned")
        more_evac = sem("more_evac")
        x_fin_clear = sem("x_fin_clear")
        x_fin_loaded = sem("x_fin_loaded")
        more_a = sem("more_a")
        more_hot = sem("more_hot")
        more_x = sem("more_x")
        more_b = sem("more_b")
        more_dhot = sem("more_dhot")
        more_sum = sem("more_sum")
        src_done = sem("src_done")
        fin_ps = sem("fin_ps")
        fin_free = sem("fin_free")
        var_ready = sem("var_ready")
        std_ready = sem("std_ready")
        out_ready = sem("out_ready")
        out_done = sem("out_done")

        block = ctx.enter_context(nc.Block())

        PAIRS = (C - 1) // 2

        def bc(ap, axis, n):
            u = ap.unsqueeze(axis)
            shape = list(u.shape)
            shape[axis] = n
            return u.to_broadcast(shape)

        def later(base, g, first):
            return nc.s_assert_within(base + (g - first + 1) * WIN, 0, NODES - 1,
                                      skip_runtime_bounds_check_because="windows are counted up to the one that holds the greatest dst")

        def further_span(eng, c):
            return nc.values_load_multi_w_load_instructions(more_tab[0:1, ds(c, 2)], engines=[eng.engine], min_val=0, max_val=C * (NODES // WIN))[1]

        def further_in(eng, span, body):
            first, last = span
            with eng.If(last > first):
                with eng.Fori(first, last) as g:
                    body(g, first)

        HALF = LO // 2
        ps_fin = ps_src[:, :, :].rearrange("p q n -> p (q n)")[:, 0:HT * P]

        def fin_bank(h, half):
            return [ps_x[:, 0, :], ps_x[:, 1, :], ps_x[:, 2, :], ps_w][h % 2 * 2 + half]

        big = spread[:, :, :, :, :, :].rearrange("p b j k l f -> p (b j k l f)").bitcast(f32)
        NF = HT * P
        sum_f = big[:, 0:HT * LO * V].rearrange("p (h l v) -> p h l v", h=HT, l=LO)
        rest_v = hi_hot[:, :, :].rearrange("p r c -> p (r c)").bitcast(f32)
        src_t = rest_v[:, 0:HCOL]
        u_all = rest_v[:, HCOL:HCOL + NF].rearrange("p (h m) -> p h m", h=HT)
        tmp_all = rest_v[:, HCOL + NF:HCOL + 2 * NF].rearrange("p (h m) -> p h m", h=HT)
        attr = rest_v[:, HCOL + 2 * NF:HCOL + 3 * NF].rearrange("p (h m) -> p h m", h=HT)
        stat = rest_v[:, HCOL + 3 * NF:]
        TAIL = NODES * F - FULLH * P * P
        TROW, TCOL = TAIL // P, TAIL % P

        TURN_AT, X_AT, ROWS_AT, SUM_AT, MERGE_AT = 2, 5, 9, 12, 14
        PIECES = {0: ["split_index", "dst_hot"], 1: ["dst_hot"] * 2, 2: ["dst_hot"] * 2, 12: ["diff"], 13: ["scale"], 14: ["left"], 15: ["parts", "spread"],
                  16: ["spread", "spread"], 17: ["same", "spread"], 18: ["spread", "spread"], 19: ["spread", "spread", "window"]}
        ROW_AT = 7
        NSTEP = 31

        def slot(b, j):
            return (b * JP + j) % RING

        @block.sync
        def _(sp):
            def load_src(c, b):
                sp.dma_start(src_i[:, b, :], src_v[ds(c, 1), :, :].rearrange("o p j -> (o p) j")).then_inc(src_loaded[b], 16)

            def load_rest(c, b):
                sp.dma_start(dst_i[:, b, :], dst_v[ds(c, 1), :, :].rearrange("o p j -> (o p) j")).then_inc(edges_loaded[b], 16)
                sp.dma_start(a2[:, b, :], a2_v[ds(c, 1), :, :].rearrange("o p j -> (o p) j")).then_inc(edges_loaded[b], 16)
                sp.dma_start(a16[:, b, :], a16_v[ds(c, 1), :, :].rearrange("o p j -> (o p) j")).then_inc(edges_loaded[b], 16)

            load_src(0, 0)
            sp.dma_start(x_rows, x.rearrange("(p n) f -> p (n f)", p=XR)).then_inc(const_loaded, 16)
            sp.dma_start(dst_all, dst.rearrange("(c e) -> c e", e=CH)).then_inc(const_loaded, 16)
            sp.dma_start(gdt[:, 0:1], dt_in.rearrange("(o t) -> o t", o=1).to_broadcast([P, 1])).then_inc(const_loaded, 16)
            sp.dma_start(gdt[:, 1:2], g_in.rearrange("(o t) -> o t", o=1).to_broadcast([P, 1])).then_inc(const_loaded, 16)
            load_src(1, 1)
            load_rest(0, 0)
            load_rest(1, 1)
            zero_rows = more_node[:, :, :].rearrange("p j n -> p (j n)").bitcast(f32)
            sp.wait_ge(scatter_zero, 1)
            assert NODES * F == XR * XC * F and XC * F <= J * WIN // 2
            sp.dma_start(pool_sum_d[0:NODES, :].rearrange("(p n) f -> p (n f)", p=XR), zero_rows[0:XR, 0:XC * F]).then_inc(scatter_clear, 16)
            sp.dma_start(pool_sum_d[NODES:NODES + P, :], zero_rows[:, 0:F]).then_inc(scatter_clear, 16)
            sp.wait_ge(x_fin_clear, 2)
            sp.dma_start(x_fin[:, 0:FULLH, :], x.rearrange("n f -> (n f)")[0:FULLH * P * P].rearrange("(h p m) -> p h m", p=P, m=P)).then_inc(x_fin_loaded, 16)
            xt = x.rearrange("n f -> (n f)")[FULLH * P * P:]
            sp.dma_start(x_fin[0:TROW, FULLH, :], xt[0:TROW * P].rearrange("(p m) -> p m", m=P)).then_inc(x_fin_loaded, 16)
            if TCOL:
                sp.dma_start(x_fin[TROW:TROW + 1, FULLH, 0:TCOL], xt[TROW * P:].rearrange("(p m) -> p m", p=1)).then_inc(x_fin_loaded, 16)
            with sp.Fori(0, PAIRS - 1) as i:
                for b in range(2):
                    sp.wait_ge(chunk_ready, i * 2 + b + 1)
                    load_src(i * 2 + (2 + b), b)
                    load_rest(i * 2 + (2 + b), b)
            sp.wait_ge(chunk_ready, C - 2)
            load_src(C - 1, 0)
            load_rest(C - 1, 0)

            sp.wait_ge(scatter_done, C * S * 16)
            sp.dma_start(pool_sum[:, 0:FULLH, :], pool_sum_d.rearrange("n f -> (n f)")[0:FULLH * P * P].rearrange("(h p m) -> p h m", p=P, m=P)).then_inc(pool_sum_loaded, 16)
            HL = -(-(NODES * F - FULLH * P * P) // P)
            sp.dma_start(pool_sum[0:HL, FULLH, :], pool_sum_d.rearrange("n f -> (n f)")[FULLH * P * P:FULLH * P * P + HL * P].rearrange("(p m) -> p m", m=P)).then_inc(pool_sum_loaded, 16)

            sp.wait_ge(out_ready, 1)
            sp.dma_start(out.rearrange("n f -> (n f)")[0:FULLH * P * P].rearrange("(h p m) -> p h m", p=P, m=P), u_all[:, 0:FULLH, :]).then_inc(out_done, 16)
            ot = out.rearrange("n f -> (n f)")[FULLH * P * P:]
            sp.dma_start(ot[0:TROW * P].rearrange("(p m) -> p m", m=P), u_all[0:TROW, FULLH, :]).then_inc(out_done, 16)
            if TCOL:
                sp.dma_start(ot[TROW * P:].rearrange("(p m) -> p m", p=1), u_all[TROW:TROW + 1, FULLH, 0:TCOL]).then_inc(out_done, 16)
            sp.wait_ge(out_done, 16 * (2 + (TCOL > 0)))

        @block.gpsimd
        def _(pool):
            nc.gpsimd.iota(col_i[:, :], pattern=[[1, P]], base=0, channel_multiplier=0).then_inc(gi_done, 1)
            nc.gpsimd.iota(row_i[:, :], pattern=[[0, 1]], base=0, channel_multiplier=1).then_inc(gi_done, 1)
            nc.gpsimd.iota(col_h[:, :], pattern=[[1, HCOL]], base=0, channel_multiplier=0,
                           allow_small_or_imprecise_dtypes=True).then_inc(gi_done, 1)

            nc.gpsimd.iota(weight_i[:, :], pattern=[[0, 1]], base=254, channel_multiplier=-2).then_inc(gi_done, 1)

            def gather(k, b):
                pool.wait_ge(src_loaded[b], k * 16 + 16)
                pool.sem_inc(gather_begun, 1)

            def gather_tiles(b, tiles):
                for j in tiles:
                    nc.gpsimd.indirect_dma_start(
                        x_src[:, b, j * F:(j + 1) * F], None, x[:, :],
                        bass.IndirectOffsetOnAxis(ap=src_i[:, b, j:j + 1], axis=0)).then_inc(gathered[b], 16)

            def scatter(c, b, s):
                if s == 0:
                    pool.wait_ge(row_ready, c + 1)
                    pool.sem_inc(rows_taken, 1)
                if not (isinstance(c, int) and c == 0 and s == 0):
                    pool.wait_ge(scatter_done, (c * S + s) * 16)
                pool.sem_inc(scatter_begun, 1)
                nc.gpsimd.indirect_dma_start(
                    pool_sum_d[:, :], bass.IndirectOffsetOnAxis(ap=row_of[:, b, s:s + 1], axis=0),
                    merged[:, b, s, 0:F], None, compute_op=ALU.add).then_inc(scatter_done, 16)

            def gather_and_scatter(c, k, b):
                gather(k, b)
                for s in range(S):
                    gather_tiles(b, range(s * J // S, (s + 1) * J // S))
                    scatter(c - 2, b, s)

            for b in range(2):
                gather(0, b)
                gather_tiles(b, range(J))
            pool.wait_ge(scatter_clear, 32)
            for b in range(2):
                gather_and_scatter(2 + b, 1, b)
            with pool.Fori(1, PAIRS - 1) as i:
                for b in range(2):
                    gather_and_scatter(i * 2 + (2 + b), i + 1, b)
            gather(PAIRS, 0)
            gather_tiles(0, range(J))
            for c, b in ((C - 3, 0), (C - 2, 1), (C - 1, 0)):
                for s in range(S):
                    scatter(c, b, s)

            pool.wait_ge(fin_count, 1)
            nc.gpsimd.tensor_tensor(attr.rearrange("p h (l f) -> p (h l) f", f=F),
                                    sum_f.rearrange("p h l v -> p (h l) v")[:, :, F + 1:2 * F + 1],
                                    bc(stat[:, 2 * HT * LO:3 * HT * LO], 2, F), ALU.mult).then_inc(attr_ready, 1)

        @block.scalar
        def _(act):
            act.wait_ge(xparts_ready, 1)
            act.dma_start(xparts_d[0:NODES, :].rearrange("(p n) q -> p (n q)", p=XR),
                          x_split.rearrange("p n k f -> p (n k f)")).then_inc(xparts_stored, 16)
            act.dma_start(xparts_d[NODES:NODES + P, :], zeros[:, 0:SPL * F]).then_inc(xparts_stored, 16)
            act.dma_start(xparts_d[NODES + P:PADN, :], zeros[0:PADN - NODES - P, 0:SPL * F]).then_inc(xparts_stored, 16)
            for n0, n1 in ((0, CLEAR[0]), (CLEAR[1], PADN)):
                nc.scalar.copy(dst_sum[:, n0:n1], zeros[:, 0:1].to_broadcast([P, n1 - n0])).then_inc(sums_clear, 1)
            act.wait_ge(xparts_stored, 48)
            act.wait_ge(tables_ready, 1)

            def window(c, b):
                base = act.value_load(base_tab[0:1, ds(c, 1)], min_val=0, max_val=NODES - 1)
                act.dma_start(xwin[:, b, :], xparts_d[ds(base, WIN), :]).then_inc(win_loaded[b], 16)

            def place_a16(c, k, b):
                act.wait_ge(edges_loaded[b], k * 48 + 48)
                nc.scalar.copy(pay[:, :, F + 1:2 * F + 1], a16[:, b, :].rearrange("p (j f) -> p j f", f=F)).then_inc(a16_copied, 1)

            def take_turned():
                for q in range(3):
                    nc.scalar.copy(node_of_dst[:, q * TPB:(q + 1) * TPB, :], turned[:, q * TPB:(q + 1) * TPB, :])
                return nc.scalar.copy(node_of_dst[:, J - 1, :], turned_last)

            def help_prepare(n, next_k, b, last, first=False):
                base = act.value_load(base_tab[0:1, ds(n, 1)], min_val=0, max_val=NODES - 1)
                span = further_span(act, n)
                act.wait_ge(hot_turned, n + 1)
                take_turned().then_inc(node_hot_ready, 1)

                def more(g, first):
                    act.wait_ge(more_x, g + 1)
                    act.dma_start(xwin_more[:, :], xparts_d[ds(later(base, g, first), WIN), :]).then_inc(more_loaded, 16)
                    act.wait_ge(more_turned, g + 1)
                    take_turned().then_inc(more_evac, 1)

                further_in(act, span, more)
                act.wait_ge(lo_ready, n + 1)
                nc.scalar.copy(lo_rows[:, :, :, :], bc(lo_hot[:, :, :], 3, F)).then_inc(lo_rows_ready, 1)
                act.wait_ge(pay_ready, n + 1)
                nc.scalar.copy(parts[:, :, 0, 0:ONE], pay[:, :, 0:ONE]).then_inc(part0_ready, 1)
                act.wait_ge(scaled_ready, n + 1)
                nc.scalar.copy(halves[:, :, 0, :], scaled[:, :, :]).then_inc(half0_ready, 1)
                act.wait_ge(left_ready, n + 1)
                nc.scalar.copy(parts[:, :, 1, 0:ONE], left[:, :, :]).then_inc(part1_ready, 1)
                if not first:
                    act.wait_ge(scatter_begun, (n - 1) * S + 1)
                act.wait_ge(merge_done, n + 1)
                nc.scalar.copy(merged[:, b, :, :], ps_merged).then_inc(merged_ready, 1)
                if not last:
                    window(n + 1, 1 - b)
                    act.wait_ge(chunk_ready, n + 1)
                    place_a16(n + 1, next_k, 1 - b)

            window(0, 0)
            place_a16(0, 0, 0)
            help_prepare(0, 0, 0, False, first=True)
            with act.Fori(0, PAIRS - 1) as i:
                help_prepare(i * 2 + 1, i + 1, 1, False)
                help_prepare(i * 2 + 2, i + 1, 0, False)
            help_prepare(C - 2, PAIRS, 1, False)
            help_prepare(C - 1, 0, 0, True)

            act.wait_ge(src_done, 1)
            act.wait_ge(hi_hot_free, C * JP + RING)
            for q in range(4):
                last = nc.scalar.copy(src_t[:, q * HB:(q + 1) * HB], ps_src[:, q, 0:HB])
            last.then_inc(src_in, 1)

            for n in range(2):
                act.wait_ge(var_ready, n + 1)
                nc.scalar.activation(stat[:, NF // F:2 * NF // F], stat[:, 0:NF // F], ACT.Sqrt, scale=1.0 / F, bias=lim[:, 3:4]).then_inc(std_ready, 1)

        @block.tensor
        def _(pe):
            pe.wait_ge(tab_sum, 1)
            nc.tensor.matmul(ps_w[0:1, 0:C], lim[0:C, 0:1], ident[0:C, 0:C], start=True, stop=True)
            nc.tensor.matmul(ps_w[0:1, P:P + C + 1], more_f[0:C, :], before[0:C, 0:C + 1], start=True, stop=True)
            nc.tensor.matmul(ps_w[:, 2 * P:2 * P + C], ones[0:C, :], base_diag[0:C, 0:C], start=True, stop=True).then_inc(tab_sum, 1)
            pe.wait_ge(gi_done, 4)
            for q in range(4):
                nc.tensor.matmul(ps_src[:, q, 0:HB], zeros[:, :], col_h[:, q * HB:(q + 1) * HB], start=True, stop=False)

            def turn(hots):
                for j in range(J):
                    last = nc.tensor.transpose(turned[:, j, :] if j < 3 * TPB else turned_last, hots[:, j, :], ident_b[:, :])
                return last

            def take_rows(window):
                for j in range(J):
                    last = nc.tensor.matmul(ps_x[:, j // PER, (j % PER) * SPL * F:(j % PER + 1) * SPL * F],
                                            node_of_dst[:, j, :], window, start=True, stop=True)
                return last

            def turn_hots(c):
                pe.wait_ge(dst_hot_ready, c * J + J)
                turn(dst_of_node).then_inc(hot_turned, 1)

            def x_of_dst(c, k, b, span):
                pe.wait_ge(win_loaded[b], k * 16 + 16)
                pe.wait_ge(node_hot_ready, c + 1)
                take_rows(xwin[:, b, :]).then_inc(x_dst_ready, 1)

                def more(g, first):
                    pe.wait_ge(more_hot, g + 1)
                    turn(more_node).then_inc(more_turned, 1)
                    pe.wait_ge(more_loaded, g * 16 + 16)
                    pe.wait_ge(more_evac, g + 1)
                    take_rows(xwin_more[:, :]).then_inc(more_x, 1)

                further_in(pe, span, more)

            def window_sums(c, span):
                pe.wait_ge(parts_ready, c + 1)

                def sums(hots):
                    for j in range(J):
                        last = nc.tensor.matmul(ps_w[0:SPL * V, 0:WIN], parts[:, j, :, :].rearrange("p k v -> p (k v)"),
                                                hots[:, j, :], start=(j == 0), stop=(j == J - 1))
                    return last

                sums(dst_of_node).then_inc(win_sum_ready, 1)

                def more(g, first):
                    pe.wait_ge(more_dhot, g + 1)
                    sums(more_node).then_inc(more_sum, 1)

                further_in(pe, span, more)

            def rows_with_src(c):
                pe.wait_ge(pay_ready, c + 1)
                for s in range(S):
                    for part in range(2):
                        last = nc.tensor.matmul(ps_rows[:, s * P:(s + 1) * P], src_f16[:, s, part:part + 1].to_broadcast([P, P]),
                                                ident_b[:, :], start=(part == 0), stop=(part == 1))
                last.then_inc(rows_of_src, 1)

            def merge(c):
                pe.wait_ge(same_ready, c + 1)
                for s in range(S):
                    for k in range(SPL):
                        nc.tensor.matmul(ps_merged[:, s, 0:F], same_src[:, s, :], parts[:, JP + s, k, 0:F], start=(k == 0), stop=(k == SPL - 1))
                    last = nc.tensor.matmul(ps_merged[:, s, F:F + 1], same_src[:, s, :], weight[:, :], start=True, stop=True)
                last.then_inc(merge_done, 1)

            def tile(c, b, j, stop):
                pe.wait_ge(hi_hot_ready, c * JP + j + 1)
                for q in range(4):
                    for k in range(HLV):
                        last = nc.tensor.matmul(ps_src[:, q, 0:HB], spread[:, b, j, k, :, :].rearrange("p l f -> p (l f)"),
                                                hi_hot[:, slot(b, j), q * HB:(q + 1) * HB], start=False, stop=stop and k == HLV - 1)
                last.then_inc(hi_hot_free, 1)

            def stage(c, k_next, b, last):
                pe.wait_ge(chunk_ready, c + 1)
                for j in range(JP):
                    if j == TURN_AT and not last:
                        span = further_span(pe, c + 1)
                    tile(c, b, j, last and j == JP - 1)
                    if j == TURN_AT and not last:
                        pe.wait_ge(merged_ready, c + 1)
                        turn_hots(c + 1)
                    if j == ROWS_AT and not last:
                        rows_with_src(c + 1)
                    if j == MERGE_AT and not last:
                        merge(c + 1)
                    if j == X_AT and not last:
                        x_of_dst(c + 1, k_next, 1 - b, span)
                    if j == SUM_AT and not last:
                        window_sums(c + 1, span)

            turn_hots(0)
            pe.wait_ge(tables_ready, 1)
            span_of_first = further_span(pe, 0)
            x_of_dst(0, 0, 0, span_of_first)
            rows_with_src(0)
            window_sums(0, span_of_first)
            merge(0)
            with pe.Fori(0, PAIRS) as i:
                stage(i * 2, i, 0, False)
                stage(i * 2 + 1, i + 1, 1, False)
            stage(C - 1, 0, 0, True)
            nc.tensor.matmul(ps_w[0:1, 0:1], ident[:, 0:1], ident[:, 0:1], start=True, stop=True).then_inc(src_done, 1)

            for h in range(HT):
                n = min(P, HCOL - h * P)
                if h >= 2:
                    pe.wait_ge(fin_free, h - 1)
                for l in range(LO):
                    last = nc.tensor.transpose(fin_bank(h, l // HALF)[0:n, (l % HALF) * SPL * V:(l % HALF + 1) * SPL * V],
                                               dst_sum[0:SPL * V, h * P * LO + l:h * P * LO + l + (n - 1) * LO + 1:LO],
                                               ident[0:SPL * V, 0:SPL * V])
                last.then_inc(fin_dst, 1)
            pe.wait_ge(src_in, 1)
            for h in range(HT):
                n = min(P, HCOL - h * P)
                last = nc.tensor.transpose(ps_fin[0:n, h * P:(h + 1) * P], src_t[:, h * P:h * P + n], ident[:, :])
            last.then_inc(fin_ps, 1)

        @block.vector
        def _(dve):
            v = nc.vector
            count = [0]

            def step(ins):
                count[0] += 1
                ins.then_inc(dve_step, 1)

            def settle(base=0):
                dve.wait_ge(dve_step, base + count[0])

            step(v.memset(zeros[:, :], 0.0))
            step(v.memset(ones[:, :], 1.0))
            v.memset(top[:, :], 0.0).then_inc(hi_hot_free, RING)
            v.memset(x_fin[:, FULLH, :], 0.0).then_inc(x_fin_clear, 1)
            v.memset(pool_sum[:, FULLH, :], 0.0).then_inc(x_fin_clear, 1)
            v.memset(more_node[:, :, :], 0.0).then_inc(scatter_zero, 1)
            step(v.memset(lim[:, :], 0.0))
            v.memset(dx[:, :], 0.0).then_inc(more_x, 1)
            v.memset(w[:, :], 0.0).then_inc(more_a, 1)
            v.memset(dst_rel[:, :], 0.0).then_inc(more_b, 1)
            dve.wait_ge(gi_done, 4)
            step(v.tensor_copy(col_f[:, :], col_i[:, :]))
            step(v.tensor_copy(row_f[:, :], row_i[:, :]))
            step(v.memset(parts[:, :, :, :], 0.0))
            step(v.tensor_scalar(weight_i[:, :], weight_i[:, :], 1.0, None, ALU.max))
            settle()
            step(v.tensor_scalar(weight_i[:, :], weight_i[:, :], float(1 << 23), None, ALU.mult))
            step(v.tensor_scalar(spare_row[:, :], row_f[:, :], float(NODES), None, ALU.add))
            settle()
            step(v.tensor_copy(weight[:, :], weight_i[:, :].bitcast(f32)))
            v.tensor_scalar(reach[:, :], weight_i[:, :].bitcast(f32), 1.75, None, ALU.mult).then_inc(weight_ready, 1)
            settle()
            step(v.memset(lim[:, 3:4], EPS))
            step(v.memset(parts[:, :, 0, ONE:ONE + 1], 1.0))
            step(v.tensor_scalar(ident[:, :], col_f[:, :], row_f[:, 0:1], None, ALU.is_equal))
            step(v.tensor_scalar(ident_b[:, :], col_f[:, :], row_f[:, 0:1], None, ALU.is_equal))
            step(v.tensor_scalar(before[:, :], col_f[:, :], row_f[:, 0:1], None, ALU.is_gt))
            settle()

            dve.wait_ge(const_loaded, 64)
            xr = x_rows.rearrange("p (n f) -> p n f", f=F)
            step(v.tensor_copy(x_split[:, :, 0, :], xr))
            settle()
            step(v.tensor_tensor(x_rest, xr, x_split[:, :, 0, :], ALU.subtract))
            settle()
            step(v.tensor_copy(x_split[:, :, 1, :], x_rest))
            settle()
            v.tensor_tensor(x_split[:, :, 2, :], x_rest, x_split[:, :, 1, :], ALU.subtract).then_inc(xparts_ready, 1)

            step(v.tensor_reduce(lim[0:C, 0:1], dst_all, AX, ALU.min))
            step(v.tensor_reduce(lim[0:C, 1:2], dst_all, AX, ALU.max))
            settle()
            step(v.tensor_tensor(more_i[0:C, 0:1], lim[0:C, 1:2], lim[0:C, 0:1], ALU.subtract))
            step(v.tensor_scalar(base_diag[0:C, 0:C], ident[0:C, 0:C], lim[0:C, 0:1], None, ALU.mult))
            settle()
            step(v.tensor_single_scalar(more_i[0:C, 1:2], more_i[0:C, 0:1], 7, ALU.arith_shift_right))
            settle()
            v.tensor_copy(more_f[0:C, :], more_i[0:C, 1:2]).then_inc(tab_sum, 1)
            dve.wait_ge(tab_sum, 2)
            step(v.tensor_copy(base_tab[0:1, 0:C], ps_w[0:1, 0:C]))
            step(v.tensor_copy(more_tab[0:1, 0:C + 1], ps_w[0:1, P:P + C + 1]))
            settle()
            v.tensor_copy(base_all[:, 0:C], ps_w[:, 2 * P:2 * P + C]).then_inc(tables_ready, 1)
            dve.wait_ge(tables_ready, 1)
            dve.wait_ge(weight_ready, 1)
            dve.wait_ge(scatter_clear, 32)
            dve.wait_ge(xparts_stored, 48)
            start = count[0]

            def x_dst_add(out_t):
                for q in range(3):
                    n = min(PER, J - q * PER)
                    yield v.tensor_reduce(out_t[:, q * PER:q * PER + n, :],
                                          ps_x[:, q, 0:n * SPL * F].rearrange("p (j k f) -> p j f k", k=SPL, f=F), AX, ALU.add)

            done = {}

            def prepare(n, k, b, piece):
                def settle_here():
                    dve.wait_ge(dve_step, start + n * NSTEP + count[0])

                if piece == "split_index":
                    count[0] = 0
                    done.clear()
                    dve.wait_ge(src_loaded[b], k * 16 + 16)
                    dve.wait_ge(edges_loaded[b], k * 48 + 48)
                    step(v.tensor_scalar(dst_rel[:, :], dst_i[:, b, :], base_all[:, ds(n, 1)], None, ALU.subtract))
                    step(v.tensor_single_scalar(lo_i[:, :], src_i[:, b, :], LO - 1, ALU.bitwise_and))
                    step(v.tensor_single_scalar(hi_i[:, :], src_i[:, b, :], LO.bit_length() - 1, ALU.logical_shift_right))
                    step(v.tensor_copy(src_f[:, b, :], src_i[:, b, JP:J]))
                    step(v.tensor_scalar(dx[:, :], a2[:, b, 0:2 * J:2], 1e-6, None, ALU.max))
                    settle_here()
                    step(v.tensor_copy(hi_f[:, b, :], hi_i[:, :]))
                    v.tensor_tensor(lo_hot[:, :, :], bc(lo_i[:, 0:JP], 2, LO), bc(col_i[:, 0:LO], 1, JP), ALU.is_equal).then_inc(lo_ready, 1)
                    step(v.tensor_scalar(src_f16[:, :, 0], hi_i[:, JP:J], float(LO), None, ALU.mult))
                    step(v.tensor_copy(src_f16[:, :, 1], lo_i[:, JP:J]))
                    step(v.reciprocal(w[:, :], dx[:, :]))
                if piece == "dst_hot":
                    first_j = done.setdefault(piece, 0)
                    done[piece] += 5
                    settle_here()
                    for j in range(first_j, first_j + 5):
                        v.tensor_scalar(dst_of_node[:, j, :], col_h[:, 0:WIN], dst_rel[:, j:j + 1], None, ALU.is_equal).then_inc(dst_hot_ready, 1)
                if piece == "diff":
                    done["span"] = span = further_span(dve, n)
                    done["base"] = dve.value_load(base_tab[0:1, ds(n, 1)], min_val=0, max_val=NODES - 1)
                    dve.wait_ge(x_dst_ready, n + 1)
                    for ins in x_dst_add(x_dst):
                        step(ins)
                    step(v.tensor_tensor(pay[:, :, F], a2[:, b, 1:2 * J:2], w[:, :], ALU.mult))
                    step(v.tensor_scalar(more_rel[:, :], dst_rel[:, :], 0.0, None, ALU.add))

                    def more(g, first):
                        settle_here()
                        dve.wait_ge(more_a, g * 5 + 1)
                        v.tensor_scalar(more_rel[:, :], more_rel[:, :], float(-WIN), None, ALU.add).then_inc(more_a, 1)
                        dve.wait_ge(more_a, g * 5 + 2)
                        v.tensor_tensor(more_node[:, :, :], bc(more_rel[:, :], 2, WIN), bc(col_f[:, 0:WIN], 1, J), ALU.is_equal).then_inc(more_hot, 1)
                        dve.wait_ge(more_x, g + 2)
                        for ins in x_dst_add(x_dst_more):
                            ins.then_inc(more_a, 1)
                        dve.wait_ge(more_a, g * 5 + 5)
                        v.tensor_tensor(x_dst[:, :, :], x_dst[:, :, :], x_dst_more[:, :, :], ALU.add).then_inc(more_a, 1)

                    further_in(dve, span, more)
                    settle_here()
                    dve.wait_ge(more_a, span[1] * 5 + 1)
                    dve.wait_ge(gathered[b], (k + 1) * 16 * J)
                    xs = x_src[:, b, :].rearrange("p (j f) -> p j f", f=F)
                    step(v.tensor_tensor(x_dst[:, :, :], x_dst[:, :, :], xs, ALU.subtract))
                    dve.wait_ge(a16_copied, n + 1)
                    settle_here()
                    v.tensor_tensor(pay[:, :, 0:F], x_dst[:, :, :], bc(w[:, :], 2, F), ALU.mult).then_inc(pay_ready, 1)
                if piece == "scale":
                    dve.wait_ge(pay_ready, n + 1)
                    step(v.tensor_reduce(top[:, :], pay[:, 0:JP, 0:F], AX, ALU.max, apply_absolute_value=True))
                    settle_here()
                    step(v.tensor_single_scalar(top[:, :].bitcast(i32), top[:, :].bitcast(i32), 0x7F800000, ALU.bitwise_and))
                    settle_here()
                    step(v.tensor_scalar(top[:, :].bitcast(i32), top[:, :].bitcast(i32), float(15 << 23), None, ALU.max))
                    settle_here()
                    step(v.tensor_scalar(scale[:, b, :].bitcast(i32), top[:, :].bitcast(i32), float(-(14 << 23)), None, ALU.add))
                    step(v.tensor_scalar(unscale[:, :].bitcast(i32), top[:, :].bitcast(i32), -1.0, float(268 << 23), ALU.mult, ALU.add))
                    settle_here()
                    v.tensor_tensor(scaled[:, :, :], pay[:, 0:JP, 0:F], bc(unscale[:, :], 2, F), ALU.mult).then_inc(scaled_ready, 1)
                if piece == "left":
                    dve.wait_ge(part0_ready, n + 1)
                    v.tensor_tensor(left[:, :, :], pay[:, :, 0:ONE], parts[:, :, 0, 0:ONE], ALU.subtract).then_inc(left_ready, 1)
                    dve.wait_ge(scaled_ready, n + 1)
                    dve.wait_ge(half0_ready, n + 1)
                    step(v.tensor_tensor(halves[:, :, 1, :], scaled[:, :, :], halves[:, :, 0, :], ALU.subtract))
                if piece == "parts":
                    dve.wait_ge(left_ready, n + 1)
                    dve.wait_ge(part1_ready, n + 1)
                    v.tensor_tensor(parts[:, :, 2, 0:ONE], left[:, :, :], parts[:, :, 1, 0:ONE], ALU.subtract).then_inc(parts_ready, 1)
                if piece == "same":
                    dve.wait_ge(rows_of_src, n + 1)
                    v.tensor_tensor(same_src[:, :, :], ps_rows.rearrange("p (s e) -> p s e", s=S), bc(src_f[:, b, :], 2, P),
                                    ALU.is_equal).then_inc(same_ready, 1)
                if piece == "spread":
                    at = done.setdefault(piece, 0)
                    done[piece] += 1
                    q, five = divmod(at, JP // 5)
                    five = slice(five * 5, five * 5 + 5)
                    if at == 0:
                        dve.wait_ge(lo_rows_ready, n + 1)
                    if at == 0 and not (isinstance(n, int) and n == 0):
                        dve.wait_ge(hi_hot_free, (n - 1) * JP + RING)
                    settle_here()
                    ins = v.tensor_tensor(spread[:, b, five, q, :, :], lo_rows[:, five, :, :], bc(halves[:, five, q, :], 2, LO), ALU.mult)
                    if at == HLV * JP // 5 - 1:
                        ins.then_inc(chunk_ready, 1)
                    else:
                        step(ins)
                if piece == "window":
                    span, base = done["span"], done["base"]
                    dve.wait_ge(win_sum_ready, n + 1)
                    win = dst_sum[0:SPL * V, ds(base, WIN)]
                    step(v.tensor_tensor(win, win, ps_w[0:SPL * V, 0:WIN], ALU.add))
                    step(v.tensor_scalar(more_rel[:, :], dst_rel[:, :], 0.0, None, ALU.add))

                    def more(g, first):
                        settle_here()
                        dve.wait_ge(more_b, g * 2 + 1)
                        v.tensor_scalar(more_rel[:, :], more_rel[:, :], float(-WIN), None, ALU.add).then_inc(more_b, 1)
                        dve.wait_ge(more_b, g * 2 + 2)
                        v.tensor_tensor(more_node[:, :, :], bc(more_rel[:, :], 2, WIN), bc(col_f[:, 0:WIN], 1, J), ALU.is_equal).then_inc(more_dhot, 1)
                        dve.wait_ge(more_sum, g + 1)
                        wn = dst_sum[0:SPL * V, ds(later(base, g, first), WIN)]
                        v.tensor_tensor(wn, wn, ps_w[0:SPL * V, 0:WIN], ALU.add).then_inc(more_b, 1)

                    further_in(dve, span, more)
                    settle_here()
                    dve.wait_ge(more_b, span[1] * 2 + 1)
                    step(v.memset(more_rel[:, :], 0.0))
                    assert count[0] == NSTEP and done["dst_hot"] == J and done["spread"] == HLV * JP // 5, (count[0], done)

            prepare(0, 0, 0, "split_index")
            for piece in ["dst_hot"] * 5:
                prepare(0, 0, 0, piece)
            dve.wait_ge(xparts_ready, 1)
            v.memset(dst_sum[:, CLEAR[0]:CLEAR[1]], 0.0).then_inc(sums_clear, 1)
            dve.wait_ge(sums_clear, 3)
            for piece in ["diff", "scale", "left", "parts"] + ["same"] + ["spread"] * (HLV * JP // 5) + ["window"]:
                prepare(0, 0, 0, piece)

            def one_hot(c, b, j):
                dve.wait_ge(hi_hot_free, c * JP + j + 1)
                v.tensor_scalar(hi_hot[:, slot(b, j), :], col_h[:, :], hi_f[:, b, j:j + 1], scale[:, b, j:j + 1],
                                ALU.is_equal, ALU.mult).then_inc(hi_hot_ready, 1)

            def rows_for_pool(c, b):
                dve.wait_ge(merged_ready, c + 1)
                v.tensor_scalar(is_later[:, :], merged[:, b, :, F], reach[:, 0:1], spare_row[:, 0:1], ALU.is_ge, ALU.mult).then_inc(later_ready, 1)
                dve.wait_ge(later_ready, c + 1)
                v.tensor_tensor(row_of[:, b, :], is_later[:, :], src_f[:, b, :], ALU.max).then_inc(row_ready, 1)

            def stage(c, k_next, b, last):
                for j in range(JP):
                    one_hot(c, b, j)
                    if j == ROW_AT:
                        rows_for_pool(c, b)
                    if not last:
                        for piece in PIECES.get(j, []):
                            prepare(c + 1, k_next, 1 - b, piece)

            with dve.Fori(0, PAIRS) as i:
                stage(i * 2, i, 0, False)
                stage(i * 2 + 1, i + 1, 1, False)
            stage(C - 1, 0, 0, True)

            fin = [0]
            fin_base = start + C * NSTEP

            def fstep(ins):
                fin[0] += 1
                ins.then_inc(dve_step, 1)

            def fsettle():
                dve.wait_ge(dve_step, fin_base + fin[0])

            dve.wait_ge(src_done, 1)
            dve.wait_ge(hi_hot_free, C * JP + RING)
            fstep(v.memset(sum_f[:, HT - 1, :, :], 0.0))
            fsettle()
            for h in range(HT):
                n = min(P, HCOL - h * P)
                dve.wait_ge(fin_dst, h + 1)
                for half in range(2):
                    last_add = v.tensor_reduce(sum_f[0:n, h, half * HALF:(half + 1) * HALF, :],
                                               fin_bank(h, half)[0:n, 0:HALF * SPL * V].rearrange("p (l k v) -> p l v k", k=SPL, v=V),
                                               AX, ALU.add)
                    fstep(last_add) if half == 0 else last_add.then_inc(fin_free, 1)
            fsettle()
            dve.wait_ge(fin_free, HT)
            dve.wait_ge(x_fin_loaded, 16 * (2 + (TCOL > 0)))

            G = HT * LO
            nodes = lambda t: t.rearrange("p h (l f) -> p (h l) f", f=F)
            sums = sum_f.rearrange("p h l v -> p (h l) v")
            u3, x3, t3, s3 = nodes(u_all), nodes(x_fin), nodes(tmp_all), ps_fin.rearrange("p (g f) -> p g f", f=F)
            var, std, cnt, mean, rstd = (stat[:, q * G:(q + 1) * G] for q in range(5))

            def op(ins):
                fstep(ins)
                fsettle()

            op(v.tensor_scalar(cnt, sums[:, :, ONE], 1.0, None, ALU.max))
            v.reciprocal(cnt, cnt).then_inc(fin_count, 1)
            op(v.tensor_scalar(gdt[:, 2:3], gdt[:, 0:1], 0.01, 2.0, ALU.max, ALU.min))
            op(v.tensor_scalar(gdt[:, 3:4], gdt[:, 2:3], -1.0, None, ALU.mult))
            op(v.tensor_scalar(mean, sums[:, :, F], gdt[:, 1:2], None, ALU.mult))
            dve.wait_ge(pool_sum_loaded, 32)
            op(v.tensor_tensor(t3, sums[:, :, 0:F], nodes(pool_sum), ALU.subtract))
            dve.wait_ge(fin_ps, 1)
            op(v.tensor_tensor(t3, t3, s3, ALU.subtract))
            op(v.tensor_tensor(t3, t3, x3, ALU.mult))
            op(v.tensor_tensor(t3, t3, bc(mean, 2, F), ALU.add))
            op(v.scalar_tensor_tensor(t3, t3, gdt[:, 3:4], x3, ALU.mult, ALU.add))
            op(v.tensor_tensor(u3, x3, t3, ALU.add))

            def layer_norm():
                op(v.tensor_reduce(mean, u3, AX, ALU.add))
                op(v.tensor_scalar(mean, mean, 1.0 / F, None, ALU.mult))
                op(v.tensor_tensor(u3, u3, bc(mean, 2, F), ALU.subtract))
                op(v.tensor_tensor(t3, u3, u3, ALU.mult))
                v.tensor_reduce(var, t3, AX, ALU.add).then_inc(var_ready, 1)

            layer_norm()
            dve.wait_ge(std_ready, 1)
            op(v.reciprocal(rstd, std))
            op(v.tensor_tensor(u3, u3, bc(rstd, 2, F), ALU.mult))
            dve.wait_ge(attr_ready, 1)
            op(v.tensor_tensor(u3, u3, nodes(attr), ALU.add))
            layer_norm()
            dve.wait_ge(std_ready, 2)
            op(v.reciprocal(rstd, std))
            v.tensor_tensor(u3, u3, bc(rstd, 2, F), ALU.mult).then_inc(out_ready, 1)


_INS = ['x', 'src', 'dst', 'edge_attr_16', 'edge_attr_2', 'L0_gnn_dt', 'L0_gnn_g']


def kernel(**inputs):
    import numpy as _np
    import concourse.bacc as _bacc
    from concourse import mybir as _mybir
    from concourse.bass_utils import run_bass_kernel_spmd as _run

    nc = _bacc.Bacc("TRN2", target_bir_lowering=False, num_devices=1)
    arrays, args = {}, []
    for name in _INS:
        a = _np.ascontiguousarray(inputs[name])
        arrays[f"in_{name}_dram"] = a
        args.append(nc.dram_tensor(f"in_{name}_dram", a.shape, _mybir.dt.from_np(a.dtype), kind="ExternalInput").ap())
    out = nc.dram_tensor("out_0_dram", inputs['x'].shape, _mybir.dt.float32, kind="ExternalOutput").ap()
    gnn_kernel(nc, *args, out)
    r = _run(nc, [arrays], core_ids=[0])
    return r.results[0]["out_0_dram"]
```
